# Optimizing a Trainium2 kernel written in Bass

```python
import numpy as np
import jax
import jax.numpy as jnp

def _softmax(x, axis=-1):
    return jax.nn.softmax(x, axis=axis)

def _gelu(x):
    return jax.nn.gelu(x, approximate=True)

def _silu(x):
    return jax.nn.silu(x)

def _sigmoid(x):
    return jax.nn.sigmoid(x)

def _layernorm(x, axis=-1, eps=1e-05):
    m = jnp.mean(x, axis=axis, keepdims=True)
    v = jnp.var(x, axis=axis, keepdims=True)
    return (x - m) / jnp.sqrt(v + eps)

def _scatter_add(tgt, idx, src, axis=0):
    return tgt.at[idx].add(src)

def _segment_sum(src, seg, n):
    return jax.ops.segment_sum(src, seg, n)
kernel_name = 'mk_dlrm_tower_d1_rec_r8_f94310'

def setup_inputs(seed: int=0):
    np.random.seed(seed)
    _w = jnp.asarray

    def _rec_inputs():
        import jax
        import jax.numpy as jnp
        _tk = jax.random.key(seed)
        ids = jnp.stack([jax.random.randint(jax.random.fold_in(_tk, 200 + f), (2048,), 0, v, jnp.int32) for f, v in enumerate([1000, 12500, 12500, 125000, 1000, 1250, 1000, 1000, 1250, 1000, 1000, 1250, 12500, 1250, 1250, 1000, 1250, 1000, 12500, 1000, 12500, 1250, 1000, 1250, 12500, 12500])], axis=1)
        tbl_0 = 0.05 * jax.random.normal(jax.random.fold_in(_tk, 500 + 0), (1000, 128), jnp.float32)
        tbl_1 = 0.05 * jax.random.normal(jax.random.fold_in(_tk, 500 + 1), (12500, 128), jnp.float32)
        tbl_2 = 0.05 * jax.random.normal(jax.random.fold_in(_tk, 500 + 2), (12500, 128), jnp.float32)
        tbl_3 = 0.05 * jax.random.normal(jax.random.fold_in(_tk, 500 + 3), (125000, 128), jnp.float32)
        tbl_4 = 0.05 * jax.random.normal(jax.random.fold_in(_tk, 500 + 4), (1000, 128), jnp.float32)
        tbl_5 = 0.05 * jax.random.normal(jax.random.fold_in(_tk, 500 + 5), (1250, 128), jnp.float32)
        tbl_6 = 0.05 * jax.random.normal(jax.random.fold_in(_tk, 500 + 6), (1000, 128), jnp.float32)
        tbl_7 = 0.05 * jax.random.normal(jax.random.fold_in(_tk, 500 + 7), (1000, 128), jnp.float32)
        tbl_8 = 0.05 * jax.random.normal(jax.random.fold_in(_tk, 500 + 8), (1250, 128), jnp.float32)
        tbl_9 = 0.05 * jax.random.normal(jax.random.fold_in(_tk, 500 + 9), (1000, 128), jnp.float32)
        tbl_10 = 0.05 * jax.random.normal(jax.random.fold_in(_tk, 500 + 10), (1000, 128), jnp.float32)
        tbl_11 = 0.05 * jax.random.normal(jax.random.fold_in(_tk, 500 + 11), (1250, 128), jnp.float32)
        tbl_12 = 0.05 * jax.random.normal(jax.random.fold_in(_tk, 500 + 12), (12500, 128), jnp.float32)
        tbl_13 = 0.05 * jax.random.normal(jax.random.fold_in(_tk, 500 + 13), (1250, 128), jnp.float32)
        tbl_14 = 0.05 * jax.random.normal(jax.random.fold_in(_tk, 500 + 14), (1250, 128), jnp.float32)
        tbl_15 = 0.05 * jax.random.normal(jax.random.fold_in(_tk, 500 + 15), (1000, 128), jnp.float32)
        tbl_16 = 0.05 * jax.random.normal(jax.random.fold_in(_tk, 500 + 16), (1250, 128), jnp.float32)
        tbl_17 = 0.05 * jax.random.normal(jax.random.fold_in(_tk, 500 + 17), (1000, 128), jnp.float32)
        tbl_18 = 0.05 * jax.random.normal(jax.random.fold_in(_tk, 500 + 18), (12500, 128), jnp.float32)
        tbl_19 = 0.05 * jax.random.normal(jax.random.fold_in(_tk, 500 + 19), (1000, 128), jnp.float32)
        tbl_20 = 0.05 * jax.random.normal(jax.random.fold_in(_tk, 500 + 20), (12500, 128), jnp.float32)
        tbl_21 = 0.05 * jax.random.normal(jax.random.fold_in(_tk, 500 + 21), (1250, 128), jnp.float32)
        tbl_22 = 0.05 * jax.random.normal(jax.random.fold_in(_tk, 500 + 22), (1000, 128), jnp.float32)
        tbl_23 = 0.05 * jax.random.normal(jax.random.fold_in(_tk, 500 + 23), (1250, 128), jnp.float32)
        tbl_24 = 0.05 * jax.random.normal(jax.random.fold_in(_tk, 500 + 24), (12500, 128), jnp.float32)
        tbl_25 = 0.05 * jax.random.normal(jax.random.fold_in(_tk, 500 + 25), (12500, 128), jnp.float32)
        _rk = jax.random.fold_in(_tk, 7)
        r_dense_features = -0.000520686 + 1.00062 * jax.random.normal(jax.random.fold_in(_rk, 101), (2048, 128), jnp.float32)
        W_top1 = 0.0405887 * jax.random.normal(jax.random.fold_in(_tk, 801), (607, 512), jnp.float32)
        W_top2 = 0.0441942 * jax.random.normal(jax.random.fold_in(_tk, 802), (512, 256), jnp.float32)
        W_top3 = 0.0625 * jax.random.normal(jax.random.fold_in(_tk, 803), (256, 1), jnp.float32)
        b_top1 = jnp.zeros((512,), jnp.float32)
        b_top2 = jnp.zeros((256,), jnp.float32)
        return (r_dense_features, ids, tbl_0, tbl_1, tbl_2, tbl_3, tbl_4, tbl_5, tbl_6, tbl_7, tbl_8, tbl_9, tbl_10, tbl_11, tbl_12, tbl_13, tbl_14, tbl_15, tbl_16, tbl_17, tbl_18, tbl_19, tbl_20, tbl_21, tbl_22, tbl_23, tbl_24, tbl_25, W_top1, b_top1, W_top2, b_top2, W_top3)
    r_dense_features, ids, tbl_0, tbl_1, tbl_2, tbl_3, tbl_4, tbl_5, tbl_6, tbl_7, tbl_8, tbl_9, tbl_10, tbl_11, tbl_12, tbl_13, tbl_14, tbl_15, tbl_16, tbl_17, tbl_18, tbl_19, tbl_20, tbl_21, tbl_22, tbl_23, tbl_24, tbl_25, W_top1, b_top1, W_top2, b_top2, W_top3 = _rec_inputs()

    def _L0_rec_setup():
        import jax, jax.numpy as jnp
        import numpy as np
        B, F, D = (2048, 26, 128)
        key = jax.random.key(seed)
        k1, k2 = jax.random.split(key)
        dense_features = jax.random.normal(k1, (B, D), dtype=jnp.float32)
        sparse_values = jax.random.normal(k2, (B, F, D), dtype=jnp.float32)
        return {'dense_features': dense_features, 'sparse_values': sparse_values}
    _L0_rec_all = _L0_rec_setup()
    _L0_rec_in = {k: v for k, v in _L0_rec_all.items() if k in ()}
    del _L0_rec_all
    return {'r_dense_features': r_dense_features, 'ids': ids, 'tbl_0': tbl_0, 'tbl_1': tbl_1, 'tbl_2': tbl_2, 'tbl_3': tbl_3, 'tbl_4': tbl_4, 'tbl_5': tbl_5, 'tbl_6': tbl_6, 'tbl_7': tbl_7, 'tbl_8': tbl_8, 'tbl_9': tbl_9, 'tbl_10': tbl_10, 'tbl_11': tbl_11, 'tbl_12': tbl_12, 'tbl_13': tbl_13, 'tbl_14': tbl_14, 'tbl_15': tbl_15, 'tbl_16': tbl_16, 'tbl_17': tbl_17, 'tbl_18': tbl_18, 'tbl_19': tbl_19, 'tbl_20': tbl_20, 'tbl_21': tbl_21, 'tbl_22': tbl_22, 'tbl_23': tbl_23, 'tbl_24': tbl_24, 'tbl_25': tbl_25, 'W_top1': W_top1, 'b_top1': b_top1, 'W_top2': W_top2, 'b_top2': b_top2, 'W_top3': W_top3}

def reference(r_dense_features, ids, tbl_0, tbl_1, tbl_2, tbl_3, tbl_4, tbl_5, tbl_6, tbl_7, tbl_8, tbl_9, tbl_10, tbl_11, tbl_12, tbl_13, tbl_14, tbl_15, tbl_16, tbl_17, tbl_18, tbl_19, tbl_20, tbl_21, tbl_22, tbl_23, tbl_24, tbl_25, W_top1, b_top1, W_top2, b_top2, W_top3):
    import jax
    import jax.numpy as jnp

    def _L0_rec_ref(dense_features, sparse_values):
        import jax, jax.numpy as jnp
        import numpy as np
        B, F, D = (2048, 26, 128)
        sd = jnp.einsum('bfd,bd->bf', sparse_values, dense_features)
        ss = jnp.einsum('bfd,bgd->bfg', sparse_values, sparse_values)
        iu, ju = jnp.triu_indices(F, k=1)
        pairs = ss[:, iu, ju]
        return jnp.concatenate([dense_features, sd, pairs], axis=1)
    e = jnp.stack([tbl_0[ids[:, 0]], tbl_1[ids[:, 1]], tbl_2[ids[:, 2]], tbl_3[ids[:, 3]], tbl_4[ids[:, 4]], tbl_5[ids[:, 5]], tbl_6[ids[:, 6]], tbl_7[ids[:, 7]], tbl_8[ids[:, 8]], tbl_9[ids[:, 9]], tbl_10[ids[:, 10]], tbl_11[ids[:, 11]], tbl_12[ids[:, 12]], tbl_13[ids[:, 13]], tbl_14[ids[:, 14]], tbl_15[ids[:, 15]], tbl_16[ids[:, 16]], tbl_17[ids[:, 17]], tbl_18[ids[:, 18]], tbl_19[ids[:, 19]], tbl_20[ids[:, 20]], tbl_21[ids[:, 21]], tbl_22[ids[:, 22]], tbl_23[ids[:, 23]], tbl_24[ids[:, 24]], tbl_25[ids[:, 25]]], axis=1)
    z = _L0_rec_ref(r_dense_features, e)
    z = z.reshape(z.shape[0], -1)
    h = jnp.concatenate([z, r_dense_features], axis=1)
    h = jnp.maximum(h @ W_top1 + b_top1, 0.0)
    h = jnp.maximum(h @ W_top2 + b_top2, 0.0)
    y = h @ W_top3
    return y

_drawn_inputs = setup_inputs


def setup_inputs(seed=0):
    import zlib

    import numpy as np

    out = dict(_drawn_inputs(seed))
    spreads = {'b_top1': (0.0, 0.1), 'b_top2': (0.0, 0.1)}
    factors = {}
    for name, (base, spread) in spreads.items():
        noise = np.random.default_rng([zlib.crc32(name.encode()), seed]).standard_normal(out[name].shape)
        drawn = base * np.exp(spread * noise) if base else spread * noise
        out[name] = jnp.asarray(drawn.astype(out[name].dtype))
    for name, factor in factors.items():
        out[name] = (out[name] * factor).astype(out[name].dtype)
    return out
```

```python
from contextlib import ExitStack

import numpy as np

import concourse.bass as bass
from concourse import mybir

BATCH, FEATS, DIM = 2048, 26, 128
HID1, HID2 = 512, 256
ONEHOT = [4, 6, 7, 9, 10]


def build(nc, dense, ids, tables, w1, b1, w2, b2, w3, y):
    fp32, fp16, bf16, i32 = mybir.dt.float32, mybir.dt.float16, mybir.dt.bfloat16, mybir.dt.int32
    ALU, ACT = mybir.AluOpType, mybir.ActivationFunctionType

    P = 128
    TILES = BATCH // P
    TQ = 4
    QUADS = TILES // TQ
    QS = TQ * P
    VECS = FEATS + 1
    GATHERED = [f for f in range(FEATS) if f not in ONEHOT]
    NG, NH = len(GATHERED), len(ONEHOT)
    ROWS = tables[ONEHOT[0]].shape[0]
    CH = 8
    RP = ROWS // CH
    OB = 3
    PARTS = 3
    assert all(tables[f].shape[0] == ROWS for f in ONEHOT) and RP * CH == ROWS and RP <= P

    SLOT_VECS = [0] + [f + 1 for f in GATHERED]
    TR_BANKS = [list(range(n, min(n + 4, len(SLOT_VECS)))) for n in range(0, len(SLOT_VECS), 4)]
    NT = len(TR_BANKS)

    def runs(slots):
        out, n = [], 0
        while n < len(slots):
            m, step = n + 1, 1
            if m < len(slots):
                step = SLOT_VECS[slots[m]] - SLOT_VECS[slots[n]]
                if step > 1 and m + 1 < len(slots) and SLOT_VECS[slots[m + 1]] - SLOT_VECS[slots[m]] != step:
                    step = 1
                else:
                    while m < len(slots) and SLOT_VECS[slots[m]] - SLOT_VECS[slots[m - 1]] == step:
                        m += 1
            out.append((n, m - n, SLOT_VECS[slots[n]], step))
            n = m
        return out

    GC = VECS - 1
    HALF = 16
    PAIRS = VECS * (VECS - 1) // 2
    KT = 3
    KP = PAIRS // KT
    M1, M2 = HID1 // P, HID2 // P
    NR = (GC + 3) // 4
    NW = NR + KT + M1 + M2
    FIRST = 2
    assert NW % 2 == 0

    DOTS_AFTER = {3: [0], 7: [1, 2], 11: [3], 15: [4, 5], 19: [6]}
    PAIRS_AFTER = {23: [0, 1], 27: [2]}
    LAYER1_AFTER = (NH - 1) * CH - 1
    LAYER2_AFTER = LAYER1_AFTER + CH // 2
    ROWS_AFTER = {LAYER1_AFTER + 2 + i: [i] for i in range(NT)}
    assert LAYER1_AFTER > 27
    SPREAD_AT = {(0, 5): 0, (1, 6): 1, (3, 0): 2}

    def pair_start(f):
        return f * (VECS - 1) - f * (f - 1) // 2

    ids_v = ids.rearrange("(p t) f -> p t f", t=TILES)
    dense_v = dense.rearrange("(p t) d -> p t d", t=TILES)

    ctx = ExitStack()
    with ctx:
        def sb(name, shape, dt=fp32):
            return ctx.enter_context(nc.sbuf_tensor(name, shape, dt))

        def bank(name):
            return ctx.enter_context(nc.psum_tensor(name, [P, 512], fp32))

        def sem(name):
            return ctx.enter_context(nc.semaphore(name))

        idx = sb("idx", [P, TQ, FEATS], i32)
        rows = sb("rows", [P, TQ, 1 + NG, DIM])
        vecT = sb("vecT", [P, QS, VECS])
        xT = sb("xT", [P, QS])
        dots = sb("dots", [P, P, GC])
        pairsT = sb("pairsT", [KP, KT, QS])
        h1 = sb("h1", [P, M1, QS])
        pairs = h1[:, :, :].rearrange("p m s -> p (m s)")[:, 0:4 * PAIRS].rearrange("p (j r) -> p j r", j=4)
        h2 = sb("h2", [P, M2, QS])
        lines = sb("lines", [33, BATCH])
        idsT, y_row = lines[0:NH, 0:BATCH // 2].bitcast(fp16), lines[32:33, :]
        w1x = sb("w1x", [P, HID1])
        w1x2 = h2[:, 0, :]
        w1p = sb("w1p", [KP, KT, HID1])
        w2_sb = sb("w2_sb", [P, M1, HID2])
        w3_sb = sb("w3_sb", [P, M2])
        b1_sb = sb("b1_sb", [P, M1])
        b2_sb = sb("b2_sb", [P, M2])
        ident = sb("ident", [P, P])
        ids_all = h1[:, 0, 0:TILES * FEATS].bitcast(i32).rearrange("p (t f) -> p t f", f=FEATS)
        ids_f = h1[:, 1, 0:TILES * NH].rearrange("p (t n) -> p t n", n=NH)
        pick = sb("pick", [NH, NH, P], fp16)
        row_i = sb("row_i", [RP, CH], i32)
        row_f = sb("row_f", [RP, CH])
        stage = dots[:, :, :].rearrange("p s f -> p (s f)")[0:RP, 0:3 * CH * DIM].rearrange("p (n x) -> p n x", n=3)
        raw, rest = stage[:, 0:2, :], stage[:, 2, :]
        split = sb("split", [RP, NH, PARTS, CH * DIM], bf16)
        onehot = sb("onehot", [RP, OB, CH, QS], bf16)

        tr_bank = [bank(f"tr_bank{n}") for n in range(2)]
        gram_bank = [bank(f"gram_bank{n}") for n in range(2)]
        work_bank = [bank(f"work_bank{n}") for n in range(2)]
        sum_bank = bank("sum_bank")
        id_bank = bank("id_bank")

        idx_loaded = [sem(f"idx_loaded{k}") for k in range(TQ)]
        dense_loaded = [sem(f"dense_loaded{k}") for k in range(TQ)]
        gathered = [sem(f"gathered{k}") for k in range(TQ)]
        raw_loaded = [sem(f"raw_loaded{n}") for n in range(2)]
        ids_loaded = sem("ids_loaded")
        weights_loaded = sem("weights_loaded")
        consts_set = sem("consts_set")
        ident_set = sem("ident_set")
        rows_numbered = sem("rows_numbered")
        row_f_set = sem("row_f_set")
        ids_cast = sem("ids_cast")
        pick_set = sem("pick_set")
        part_cast = sem("part_cast")
        part_taken = sem("part_taken")
        w1x_summed = sem("w1x_summed")
        tr_filled, tr_drained = sem("tr_filled"), sem("tr_drained")
        gram_filled, gram_drained = sem("gram_filled"), sem("gram_drained")
        work_filled, work_drained = sem("work_filled"), sem("work_drained")
        sum_filled, sum_drained = sem("sum_filled"), sem("sum_drained")
        id_filled = sem("id_filled")
        y_filled, y_drained = sem("y_filled"), sem("y_drained")
        slot_turned = sem("slot_turned")
        onehot_set = sem("onehot_set")
        y_stored = sem("y_stored")

        block = ctx.enter_context(nc.Block())

        @block.sync
        def _(sp):
            sp.dma_start(idx[:, 0, :], ids_v[:, 0, :]).then_inc(idx_loaded[0], 16)
            sp.dma_start(ids_all, ids_v).then_inc(ids_loaded, 16)
            for n in range(2):
                sp.dma_start(raw[:, n, :], tables[ONEHOT[n]].rearrange("(p c) d -> p (c d)", c=CH)
                             ).then_inc(raw_loaded[n], 16)
            for k in range(1, TQ):
                sp.dma_start(idx[:, k, :], ids_v[:, k, :]).then_inc(idx_loaded[k], 16)
            for k in range(TQ):
                sp.dma_start(rows[:, k, 0, :], dense_v[:, k, :]).then_inc(dense_loaded[k], 16)
            for n in range(2, NH):
                sp.wait_ge(part_taken, 2 * (n - 2) + 1)
                sp.dma_start(raw[:, n % 2, :], tables[ONEHOT[n]].rearrange("(p c) d -> p (c d)", c=CH)
                             ).then_inc(raw_loaded[n % 2], 16)
            sp.dma_start(w1x[:], w1[0:P, :]).then_inc(weights_loaded, 16)
            sp.dma_start(w1x2, w1[P + PAIRS:P + PAIRS + P, :]).then_inc(weights_loaded, 16)
            sp.dma_start(w1p[:], w1[P:P + PAIRS, :].rearrange("(k p) n -> p k n", k=KT)
                         ).then_inc(weights_loaded, 16)
            sp.dma_start(w2_sb[:], w2.rearrange("(k p) n -> p k n", p=P)).then_inc(weights_loaded, 16)
            with nc.allow_non_contiguous_dma(reason="biases and the last layer: 1 K elements in all"):
                sp.dma_start(w3_sb[:], w3.rearrange("(k p) o -> p (k o)", p=P)).then_inc(weights_loaded, 16)
                sp.dma_start(b1_sb[:], b1.rearrange("(k p) -> p k", p=P)).then_inc(weights_loaded, 16)
                sp.dma_start(b2_sb[:], b2.rearrange("(k p) -> p k", p=P)).then_inc(weights_loaded, 16)
            with sp.Fori(1, QUADS) as q:
                for k in range(TQ):
                    sp.wait_ge(gathered[k], 16 * NG * q)
                    sp.dma_start(idx[:, k, :], ids_v[:, bass.ds(TQ * q + k, 1), :]
                                 .rearrange("p a f -> p (a f)")).then_inc(idx_loaded[k], 16)
                    sp.wait_ge(tr_filled, FIRST + NT * TQ * (q - 1) + NT * (k + 1))
                    sp.dma_start(rows[:, k, 0, :], dense_v[:, bass.ds(TQ * q + k, 1), :]
                                 .rearrange("p a f -> p (a f)")).then_inc(dense_loaded[k], 16)
            sp.wait_ge(y_drained, 1 + QUADS + 1)
            sp.dma_start(y.rearrange("b o -> o b"), y_row).then_inc(y_stored, 16)
            sp.wait_ge(y_stored, 16)

        @block.gpsimd
        def _(pool):
            nc.gpsimd.memset(ident[:], 0.0).then_inc(consts_set, 1)
            pool.wait_ge(consts_set, 1)
            nc.gpsimd.affine_select(out=ident[:], in_=ident[:], compare_op=ALU.not_equal, fill=1.0, base=0,
                                    pattern=[[-1, P]], channel_multiplier=1).then_inc(ident_set, 1)
            nc.gpsimd.iota(row_i[:], pattern=[[1, CH]], base=0, channel_multiplier=CH).then_inc(rows_numbered, 1)

            def gather(k):
                for n, f in enumerate(GATHERED):
                    nc.gpsimd.indirect_dma_start(
                        rows[:, k, 1 + n, :], None, tables[f],
                        bass.IndirectOffsetOnAxis(idx[:, k, f:f + 1], 0)).then_inc(gathered[k], 16)

            for k in range(TQ):
                pool.wait_ge(idx_loaded[k], 16)
                gather(k)
            with pool.Fori(1, QUADS) as q:
                for k in range(TQ):
                    pool.wait_ge(idx_loaded[k], 16 * q + 16)
                    pool.wait_ge(tr_filled, FIRST + NT * TQ * (q - 1) + NT * (k + 1))
                    pool.sem_inc(slot_turned, 1)
                    gather(k)

        @block.vector
        def _(dve):
            for n in range(FIRST):
                nc.vector.memset(gram_bank[n][:], 0.0).then_inc(gram_drained, 1)
            dve.wait_ge(ids_loaded, 16)
            for n, f in enumerate(ONEHOT):
                last = nc.vector.tensor_copy(ids_f[:, :, n], ids_all[:, :, f])
            last.then_inc(ids_cast, 1)
            dve.wait_ge(rows_numbered, 1)
            nc.vector.tensor_copy(row_f[:], row_i[:]).then_inc(row_f_set, 1)
            dve.wait_ge(row_f_set, 1)

            def wait_ids(q, n, sums):
                dve.wait_ge(id_filled, NH * q + n + 1)
                if not isinstance(sums, int) or sums > 0:
                    dve.wait_ge(sum_filled, sums)

            def set_onehot(n, chunks):
                for c in chunks:
                    last = nc.vector.tensor_scalar(onehot[:, n % OB, c, :], id_bank[0:RP, :], row_f[:, c:c + 1],
                                                   None, ALU.is_equal)
                if c == CH - 1:
                    last.then_inc(onehot_set, 1)

            for n in range(NH):
                dve.wait_ge(part_cast, 2 * n + 1)
                if n:
                    dve.wait_ge(part_taken, 2 * n)
                nc.vector.tensor_tensor(rest, raw[:, n % 2, :], split[:, n, 0, :],
                                        ALU.subtract).then_inc(part_taken, 1)
                wait_ids(0, n, max(n + 1 - OB, 0))
                set_onehot(n, range(CH // 2))
                dve.wait_ge(part_cast, 2 * n + 2)
                dve.wait_ge(part_taken, 2 * n + 1)
                nc.vector.tensor_tensor(split[:, n, 2, :], rest, split[:, n, 1, :],
                                        ALU.subtract).then_inc(part_taken, 1)
                set_onehot(n, range(CH // 2, CH))
            dve.wait_ge(weights_loaded, 16 * 7)
            nc.vector.tensor_tensor(w1x[:], w1x[:], w1x2, ALU.add).then_inc(w1x_summed, 1)
            with dve.Fori(1, QUADS) as q:
                for n in range(NH):
                    wait_ids(q, n, NH * q + max(n + 1 - OB, 0))
                    set_onehot(n, range(CH))

        @block.scalar
        def _(act):
            act.wait_ge(ident_set, 1)
            for n in range(NH):
                last = nc.scalar.copy(pick[:, n, :], ident[0:NH, n:n + 1].broadcast_to([NH, P]))
            last.then_inc(pick_set, 1)
            act.sem_inc(y_drained, 1)
            for n in range(FIRST):
                for bank_of, filled, drained, q in ((tr_bank, tr_filled, tr_drained, n),
                                                    (work_bank, work_filled, work_drained, FIRST + n)):
                    act.wait_ge(filled, n + 1)
                    nc.scalar.copy(idsT[:, q * QS:(q + 1) * QS], bank_of[n][0:NH, :]).then_inc(drained, 1)

            def cast_parts(n):
                act.wait_ge(raw_loaded[n % 2], 16 * (n // 2 + 1))
                nc.scalar.copy(split[:, n, 0, :], raw[:, n % 2, :]).then_inc(part_cast, 1)
                act.wait_ge(part_taken, 2 * n + 1)
                nc.scalar.copy(split[:, n, 1, :], rest).then_inc(part_cast, 1)

            def drain_sum(use, n):
                act.wait_ge(sum_filled, use + 1)
                nc.scalar.copy(vecT[:, :, ONEHOT[n] + 1], sum_bank[:]).then_inc(sum_drained, 1)

            def drain_rows(q, k, i):
                slots, src = TR_BANKS[i], tr_bank[(NT * k + i) % 2]
                act.wait_ge(tr_filled, FIRST + NT * TQ * q + NT * k + i + 1)
                if i == 0:
                    nc.scalar.copy(xT[:, :].rearrange("d (j t i) -> d t j i", j=4, t=TQ)[:, k],
                                   src[:, 0:P].rearrange("d (j i) -> d j i", j=4))
                for first, count, vec, step in runs(slots):
                    last = nc.scalar.copy(
                        vecT[:, k * P:(k + 1) * P, vec:vec + step * (count - 1) + 1:step]
                        .rearrange("d s v -> d v s"),
                        src[:, first * P:(first + count) * P].rearrange("d (v s) -> d v s", v=count))
                last.then_inc(tr_drained, 1)

            def drain_tile(q, k, next_rows):
                for part in range(8):
                    if part % 4 == 3:
                        drain_gram(q, k, part // 4)
                    if next_rows and part < NT:
                        drain_rows(q, k + 1, part)

            def drain_gram(q, k, h):
                act.wait_ge(gram_filled, 2 * TQ * q + 2 * k + h + 1)
                at = k * 2 * HALF + h * HALF
                nc.scalar.copy(dots[:, at:at + HALF, :],
                               gram_bank[h][:, 0:HALF * GC].rearrange("p (i f) -> p i f", f=GC)
                               ).then_inc(gram_drained, 1)

            def drain_dots(first, groups, r):
                act.wait_ge(work_filled, first + r + 1)
                src = work_bank[r % 2][0:groups, :].rearrange("p (f j g) -> p f j g", f=4, j=4)
                for f in range(4 * r, min(4 * r + 4, GC)):
                    last = nc.scalar.copy(pairs[0:groups, :, pair_start(f):pair_start(f) + GC - f],
                                          src[:, f % 4, :, f:GC])
                last.then_inc(work_drained, 1)

            def drain_pairs(first, t0, nt, b):
                use = NR + b
                act.wait_ge(work_filled, first + use + 1)
                nc.scalar.copy(pairsT[:, b, :].rearrange("r (j t i) -> r j t i", j=4, t=TQ)[:, :, t0:t0 + nt],
                               work_bank[use % 2][0:KP, 0:nt * P].rearrange("r (j t i) -> r j t i", j=4, t=nt)
                               ).then_inc(work_drained, 1)

            def drain_layer1(first, nt):
                for m in range(M1):
                    use = NR + KT + m
                    act.wait_ge(work_filled, first + use + 1)
                    nc.scalar.activation(h1[:, m, 0:nt * P], work_bank[use % 2][:, 0:nt * P], ACT.Relu,
                                         bias=b1_sb[:, m:m + 1]).then_inc(work_drained, 1)

            def drain_layer2(first, nt):
                for m in range(M2):
                    use = NR + KT + M1 + m
                    act.wait_ge(work_filled, first + use + 1)
                    nc.scalar.activation(h2[:, m, 0:nt * P], work_bank[use % 2][:, 0:nt * P], ACT.Relu,
                                         bias=b2_sb[:, m:m + 1]).then_inc(work_drained, 1)

            def drain_y(tile, nt, use):
                act.wait_ge(y_filled, use + 1)
                nc.scalar.copy(y_row.rearrange("o (j i t) -> o j t i", j=4, t=TILES)[:, :, bass.ds(tile, nt), :],
                               id_bank[32:33, 0:nt * P].rearrange("o (j t i) -> o j t i", j=4, t=nt)
                               ).then_inc(y_drained, 1)

            def quad(q):
                for k in range(TQ):
                    drain_tile(q, k, k + 1 < TQ)
                first, sums = FIRST + NW * q, NH * (q + 1)
                for at in range(NH * CH):
                    if at % CH == CH - 1:
                        drain_sum(sums + at // CH, at // CH)
                    for r in DOTS_AFTER.get(at, []):
                        drain_dots(first, P, r)
                    for b in PAIRS_AFTER.get(at, []):
                        drain_pairs(first, 0, TQ, b)
                    for i in ROWS_AFTER.get(at, []):
                        drain_rows(q + 1, 0, i)
                    if at == LAYER1_AFTER:
                        drain_layer1(first, TQ)
                    if at == LAYER2_AFTER:
                        drain_layer2(first, TQ)
                drain_y(TQ * q, TQ, q)

            def finish(q, t0, nt, first, use):
                for r in range(NR):
                    drain_dots(first, nt * P // 4, r)
                for b in range(KT):
                    drain_pairs(first, t0, nt, b)
                drain_layer1(first, nt)
                drain_layer2(first, nt)
                drain_y(TQ * q + t0, nt, use)

            for n in range(NH):
                cast_parts(n)
                if n:
                    drain_sum(n - 1, n - 1)
            drain_sum(NH - 1, NH - 1)
            act.wait_ge(weights_loaded, 16 * 7)
            for i in range(NT):
                drain_rows(0, 0, i)
            with act.Fori(0, QUADS - 1) as q:
                quad(q)
            q = QUADS - 1
            for k in range(TQ - 1):
                drain_tile(q, k, k + 2 < TQ)
            finish(q, 0, TQ - 1, FIRST + NW * q, q)
            for i in range(NT):
                drain_rows(q, TQ - 1, i)
            drain_tile(q, TQ - 1, False)
            finish(q, TQ - 1, 1, FIRST + NW * (q + 1), q + 1)

        @block.tensor
        def _(pe):
            pe.wait_ge(ident_set, 1)
            pe.wait_ge(ids_cast, 1)
            for n in range(FIRST):
                for bank_of, filled, q in ((tr_bank, tr_filled, n), (work_bank, work_filled, FIRST + n)):
                    for k in range(TQ):
                        last = nc.tensor.transpose(bank_of[n][0:NH, k * P:(k + 1) * P], ids_f[:, TQ * q + k, :],
                                                   ident[:])
                    last.then_inc(filled, 1)
            pe.wait_ge(pick_set, 1)
            pe.wait_ge(tr_drained, FIRST)
            pe.wait_ge(work_drained, FIRST)

            def spread_ids(q, n):
                nc.tensor.matmul(id_bank[:, :], pick[:, n, :], idsT[:, bass.ds(q * QS, QS)],
                                 start=True, stop=True).then_inc(id_filled, 1)

            def lookup(q, use, sums, at, ahead, spread_at, spread_from):
                n, c = at // CH, at % CH
                if c == 0:
                    pe.wait_ge(onehot_set, use + n + 1)
                    pe.wait_ge(sum_drained, sums + n)
                spread = n + ahead if c == spread_at and spread_from <= n + ahead < NH else None
                if spread is not None:
                    pe.wait_ge(onehot_set, use + spread)
                for part in range(PARTS):
                    last = nc.tensor.matmul(sum_bank[:, :], split[:, n, part, c * DIM:(c + 1) * DIM],
                                            onehot[:, n % OB, c, :],
                                            start=(c == 0 and part == 0), stop=(c == CH - 1 and part == PARTS - 1))
                if c == CH - 1:
                    last.then_inc(sum_filled, 1)
                if spread is not None:
                    spread_ids(q, spread)

            def transpose_rows(q, k, i):
                if i == 0:
                    pe.wait_ge(dense_loaded[k], 16 * q + 16)
                    pe.wait_ge(gathered[k], 16 * NG * q + 16 * NG)
                use = NT * k + i
                pe.wait_ge(tr_drained, FIRST + NT * TQ * q + use - 1)
                for s in TR_BANKS[i]:
                    last = nc.tensor.transpose(tr_bank[use % 2][:, (s % 4) * P:(s % 4 + 1) * P],
                                               rows[:, k, s, :], ident[:])
                last.then_inc(tr_filled, 1)

            def gram_tile(q, k, interleave, spreads=False):
                pe.wait_ge(tr_drained, FIRST + NT * TQ * q + NT * (k + 1))
                for part in range(8):
                    h, i0 = part // 4, part % 4 * 4
                    if i0 == 0:
                        pe.wait_ge(gram_drained, FIRST + 2 * TQ * q + 2 * k + h - 1)
                    n = SPREAD_AT.get((k, part)) if spreads else None
                    if n == 0:
                        pe.wait_ge(y_drained, q + 1)
                    elif n is not None:
                        pe.wait_ge(onehot_set, NH * (q + 1) + n)
                    for i in range(i0, i0 + 4):
                        for j in range(4):
                            s = k * P + 32 * j + h * HALF + i
                            last = nc.tensor.matmul(gram_bank[h][32 * j:32 * j + GC, i * GC:(i + 1) * GC],
                                                    vecT[:, s, 1:VECS], vecT[:, s, 0:GC], start=True, stop=True)
                    if i0 == 12:
                        last.then_inc(gram_filled, 1)
                    if n is not None:
                        spread_ids(q + 1, n)
                    if interleave and part < NT:
                        transpose_rows(q, k + 1, part)

            def free_work(first, use):
                pe.wait_ge(work_drained, first + use - 1)

            def transpose_dots(first, t0, nt, r):
                free_work(first, r)
                for f in range(4 * r, min(4 * r + 4, GC)):
                    last = nc.tensor.transpose(work_bank[r % 2][0:32 * nt, (f % 4) * P:(f % 4 + 1) * P],
                                               dots[:, 32 * t0:32 * (t0 + nt), f], ident[:])
                last.then_inc(work_filled, 1)

            def transpose_pairs(first, nt, b):
                use, n = NR + b, 32 * nt
                if b == 0:
                    pe.wait_ge(work_drained, first + NR)
                free_work(first, use)
                for j in range(4):
                    last = nc.tensor.transpose(work_bank[use % 2][0:KP, j * n:(j + 1) * n],
                                               pairs[0:n, j, b * KP:(b + 1) * KP], ident[0:n, 0:n])
                last.then_inc(work_filled, 1)

            def layer1(first, t0, nt):
                pe.wait_ge(work_drained, first + NR + KT)
                xT_v = xT[:, :].rearrange("d (j t i) -> d j t i", j=4, t=TQ)[:, :, t0:t0 + nt]
                for m in range(M1):
                    use = NR + KT + m
                    free_work(first, use)
                    cols = slice(m * P, (m + 1) * P)
                    out = work_bank[use % 2][:, 0:nt * P].rearrange("u (j t i) -> u j t i", j=4, t=nt)
                    nc.tensor.matmul(out, w1x[:, cols], xT_v, start=True, stop=False)
                    for b in range(KT):
                        pT_v = pairsT[:, b, :].rearrange("r (j t i) -> r j t i", j=4, t=TQ)[:, :, t0:t0 + nt]
                        last = nc.tensor.matmul(out, w1p[:, b, cols], pT_v, start=False, stop=(b == KT - 1))
                    last.then_inc(work_filled, 1)

            def layer2(first, nt):
                pe.wait_ge(work_drained, first + NR + KT + M1)
                for m in range(M2):
                    use = NR + KT + M1 + m
                    free_work(first, use)
                    for b in range(M1):
                        last = nc.tensor.matmul(work_bank[use % 2][:, 0:nt * P], w2_sb[:, b, m * P:(m + 1) * P],
                                                h1[:, b, 0:nt * P], start=(b == 0), stop=(b == M1 - 1))
                    last.then_inc(work_filled, 1)

            def layer3(first, nt):
                pe.wait_ge(work_drained, first + NW)
                for b in range(M2):
                    last = nc.tensor.matmul(id_bank[32:33, 0:nt * P], w3_sb[:, b:b + 1], h2[:, b, 0:nt * P],
                                            start=(b == 0), stop=(b == M2 - 1))
                last.then_inc(y_filled, 1)

            def quad(q):
                pe.wait_ge(sum_drained, NH * (q + 1))
                for k in range(TQ):
                    gram_tile(q, k, interleave=k + 1 < TQ, spreads=True)
                first, sums = FIRST + NW * q, NH * (q + 1)
                for at in range(NH * CH):
                    lookup(q + 1, NH * (q + 1), sums, at, ahead=2, spread_at=CH // 2,
                           spread_from=len(SPREAD_AT))
                    for r in DOTS_AFTER.get(at, []):
                        if r == 0:
                            pe.wait_ge(gram_drained, FIRST + 2 * TQ * (q + 1))
                        transpose_dots(first, 0, TQ, r)
                    for b in PAIRS_AFTER.get(at, []):
                        transpose_pairs(first, TQ, b)
                    for i in ROWS_AFTER.get(at, []):
                        transpose_rows(q + 1, 0, i)
                    if at == LAYER1_AFTER:
                        layer1(first, 0, TQ)
                    if at == LAYER2_AFTER:
                        layer2(first, TQ)
                layer3(first, TQ)

            def finish(q, t0, nt, first, use):
                pe.wait_ge(gram_drained, FIRST + 2 * TQ * q + 2 * (t0 + nt))
                for r in range(NR):
                    transpose_dots(first, t0, nt, r)
                for b in range(KT):
                    transpose_pairs(first, nt, b)
                layer1(first, t0, nt)
                layer2(first, nt)
                pe.wait_ge(y_drained, use + 1)
                layer3(first, nt)

            spread_ids(0, 0)
            for n in range(NH):
                pe.wait_ge(part_taken, 2 * n + 2)
                for c in range(CH):
                    lookup(0, 0, 0, n * CH + c, ahead=1, spread_at=CH // 2, spread_from=1)
            pe.wait_ge(w1x_summed, 1)
            for i in range(NT):
                transpose_rows(0, 0, i)
            with pe.Fori(0, QUADS - 1) as q:
                quad(q)
            q = QUADS - 1
            pe.wait_ge(sum_drained, NH * (q + 1))
            for k in range(TQ - 1):
                gram_tile(q, k, interleave=k + 2 < TQ)
            finish(q, 0, TQ - 1, FIRST + NW * q, q)
            for i in range(NT):
                transpose_rows(q, TQ - 1, i)
            gram_tile(q, TQ - 1, interleave=False)
            finish(q, TQ - 1, 1, FIRST + NW * (q + 1), q + 1)


_INS = (["r_dense_features", "ids"] + [f"tbl_{i}" for i in range(FEATS)]
        + ["W_top1", "b_top1", "W_top2", "b_top2", "W_top3"])


def kernel(**inputs):
    import concourse.bacc as bacc
    from concourse.bass_utils import run_bass_kernel_spmd

    nc = bacc.Bacc("TRN2", target_bir_lowering=False, num_devices=1)
    arrays, aps = {}, []
    for name in _INS:
        a = np.ascontiguousarray(inputs[name])
        arrays[f"in_{name}"] = a
        aps.append(nc.dram_tensor(f"in_{name}", a.shape, mybir.dt.from_np(a.dtype), kind="ExternalInput").ap())
    y = nc.dram_tensor("out_y", (BATCH, 1), mybir.dt.float32, kind="ExternalOutput").ap()
    build(nc, aps[0], aps[1], aps[2:2 + FEATS], *aps[2 + FEATS:], y)
    return run_bass_kernel_spmd(nc, [arrays], core_ids=[0]).results[0]["out_y"]
```

```python
from contextlib import ExitStack

import numpy as np

import concourse.bass as bass
from concourse import mybir

BATCH, FEATS, DIM = 2048, 26, 128
HID1, HID2 = 512, 256
ONEHOT = [4, 6, 7, 9, 10, 15]


def build(nc, dense, ids, tables, w1, b1, w2, b2, w3, y):
    fp32, fp16, bf16, i32 = mybir.dt.float32, mybir.dt.float16, mybir.dt.bfloat16, mybir.dt.int32
    ALU, ACT = mybir.AluOpType, mybir.ActivationFunctionType

    P = 128
    TILES = BATCH // P
    TQ = 4
    QUADS = TILES // TQ
    QS = TQ * P
    VECS = FEATS + 1
    GATHERED = [f for f in reversed(range(FEATS)) if f not in ONEHOT]
    NG, NH = len(GATHERED), len(ONEHOT)
    ROWS = tables[ONEHOT[0]].shape[0]
    CH = 8
    RP = ROWS // CH
    OB = 2
    EARLY = 2
    PARTS = 3
    assert all(tables[f].shape[0] == ROWS for f in ONEHOT) and RP * CH == ROWS and RP <= P

    def place(v):
        return VECS - 1 - v

    SLOT_PLACES = [place(f + 1) for f in GATHERED] + [place(0)]
    TR_BANKS = [list(range(n, min(n + 4, NG + 1))) for n in range(0, NG + 1, 4)]
    NT = len(TR_BANKS)

    def runs(slots):
        out, n = [], 0
        while n < len(slots):
            m, step = n + 1, 1
            if m < len(slots):
                step = SLOT_PLACES[slots[m]] - SLOT_PLACES[slots[n]]
                if step > 1 and m + 1 < len(slots) and SLOT_PLACES[slots[m + 1]] - SLOT_PLACES[slots[m]] != step:
                    step = 1
                else:
                    while m < len(slots) and SLOT_PLACES[slots[m]] - SLOT_PLACES[slots[m - 1]] == step:
                        m += 1
            out.append((n, m - n, SLOT_PLACES[slots[n]], step))
            n = m
        return out

    GC = VECS - 1
    HALF = 16
    BL = 32
    PAIRS = VECS * (VECS - 1) // 2
    KT = 3
    KP = PAIRS // KT
    M1, M2 = HID1 // P, HID2 // P
    L1, L2 = TQ, TQ + M1
    NW = L2 + M2
    FIRST = 2
    assert NW % 2 == 0

    ROWS_AT = {2: 0, 3: EARLY * CH - (NT + 1) // 2}
    SPREAD_AFTER = {CH: 3, 2 * CH + 1: 4, **{(n - 1) * CH + 2: n for n in range(5, NH)}}
    PAIRS_AFTER = {CH - 1: [0], **{(EARLY + k) * CH - 1: [k] for k in range(1, TQ)}}

    ROWS_FIRST = {NH - 3: range(0, 4), NH - 2: range(4, 8), NH - 1: range(8, 2 * NT)}

    PAD = BL - GC

    def pairs_of(c, n):
        end = PAD + PAIRS - c * (c + 1) // 2
        return slice(end - 1, end - 1 - n if end > n else None, -1)

    ids_v = ids.rearrange("(p t) f -> p t f", t=TILES)
    dense_v = dense.rearrange("(p t) d -> p t d", t=TILES)

    ctx = ExitStack()
    with ctx:
        def sb(name, shape, dt=fp32):
            return ctx.enter_context(nc.sbuf_tensor(name, shape, dt))

        def bank(name):
            return ctx.enter_context(nc.psum_tensor(name, [P, 512], fp32))

        def sem(name):
            return ctx.enter_context(nc.semaphore(name))

        idx = sb("idx", [P, TQ, FEATS], i32)
        rows = sb("rows", [P, TQ, NG + 1, DIM])
        vecT = sb("vecT", [P, QS, VECS])
        xT = sb("xT", [P, QS])
        dots = sb("dots", [P, 2, BL, GC])
        pairs = sb("pairs", [P, TQ, PAD + PAIRS])
        pairsT = sb("pairsT", [P, KT, QS])
        held = sb("held", [P, EARLY, P])
        h1 = sb("h1", [P, M1, QS])
        h2 = sb("h2", [P, M2, QS])
        lines = sb("lines", [33, BATCH])
        idsT, y_row = lines[0:NH, 0:(BATCH + QS) // 2].bitcast(fp16), lines[32:33, :]
        w1x = sb("w1x", [P, HID1])
        w1x2 = h2[:, 0, :]
        w1p = sb("w1p", [KP, KT, HID1])
        w2_sb = sb("w2_sb", [P, M1, HID2])
        w3_sb = sb("w3_sb", [P, M2])
        b1_sb = sb("b1_sb", [P, M1])
        b2_sb = sb("b2_sb", [P, M2])
        ident = sb("ident", [P, P])
        ids_all = h1[:, 0, 0:TILES * FEATS].bitcast(i32).rearrange("p (t f) -> p t f", f=FEATS)
        ids_f = h1[:, 1, 0:TILES * NH].rearrange("p (t n) -> p t n", n=NH)
        pick = sb("pick", [NH, NH, P], fp16)
        row_i = sb("row_i", [RP, CH], i32)
        row_f = sb("row_f", [RP, CH])
        raw = [pairsT[:, :, :].rearrange("p k s -> p (k s)")[0:RP, 0:CH * DIM],
               h1[:, 2:4, :].rearrange("p m s -> p (m s)")[0:RP, 0:CH * DIM]]
        rest = pairs[:, :, :].rearrange("p t m -> p (t m)")[0:RP, 0:CH * DIM]
        split = sb("split", [RP, NH, PARTS, CH * DIM], bf16)
        onehot = sb("onehot", [RP, OB, CH, QS], bf16)

        tr_bank = [bank(f"tr_bank{n}") for n in range(2)]
        gram_bank = [bank(f"gram_bank{n}") for n in range(2)]
        work_bank = [bank(f"work_bank{n}") for n in range(2)]
        sum_bank = bank("sum_bank")
        id_bank = bank("id_bank")

        idx_loaded = [sem(f"idx_loaded{k}") for k in range(TQ)]
        dense_loaded = [sem(f"dense_loaded{k}") for k in range(TQ)]
        gathered = [sem(f"gathered{k}") for k in range(TQ)]
        raw_loaded = [sem(f"raw_loaded{n}") for n in range(2)]
        ids_loaded = sem("ids_loaded")
        weights_loaded = sem("weights_loaded")
        consts_set = sem("consts_set")
        ident_set = sem("ident_set")
        rows_numbered = sem("rows_numbered")
        row_f_set = sem("row_f_set")
        ids_cast = sem("ids_cast")
        no_ids_set = sem("no_ids_set")
        pick_set = sem("pick_set")
        part_cast = sem("part_cast")
        part_taken = sem("part_taken")
        w1x_summed = sem("w1x_summed")
        tr_filled, tr_drained = sem("tr_filled"), sem("tr_drained")
        gram_filled, gram_drained = sem("gram_filled"), sem("gram_drained")
        work_filled, work_drained = sem("work_filled"), sem("work_drained")
        sum_drained = sem("sum_drained")
        id_filled = sem("id_filled")
        y_filled, y_drained = sem("y_filled"), sem("y_drained")
        slot_turned = sem("slot_turned")
        all_turned = sem("all_turned")
        pairs_set, column_turned = sem("pairs_set"), sem("column_turned")
        onehot_set, chunk_done = sem("onehot_set"), sem("chunk_done")
        y_stored = sem("y_stored")

        block = ctx.enter_context(nc.Block())

        @block.sync
        def _(sp):
            sp.dma_start(idx[:, 0, :], ids_v[:, 0, :]).then_inc(idx_loaded[0], 16)
            sp.dma_start(ids_all, ids_v).then_inc(ids_loaded, 16)
            for n in range(2):
                sp.dma_start(raw[n], tables[ONEHOT[n]].rearrange("(p c) d -> p (c d)", c=CH)
                             ).then_inc(raw_loaded[n], 16)
            for k in range(1, TQ):
                sp.dma_start(idx[:, k, :], ids_v[:, k, :]).then_inc(idx_loaded[k], 16)
            for k in range(TQ):
                sp.dma_start(rows[:, k, NG, :], dense_v[:, k, :]).then_inc(dense_loaded[k], 16)
            for n in range(2, NH):
                sp.wait_ge(part_taken, 2 * (n - 2) + 1)
                sp.dma_start(raw[n % 2], tables[ONEHOT[n]].rearrange("(p c) d -> p (c d)", c=CH)
                             ).then_inc(raw_loaded[n % 2], 16)
            sp.dma_start(w1x[:], w1[0:P, :]).then_inc(weights_loaded, 16)
            sp.dma_start(w1x2, w1[P + PAIRS:P + PAIRS + P, :]).then_inc(weights_loaded, 16)
            sp.dma_start(w1p[:], w1[P:P + PAIRS, :].rearrange("(k p) n -> p k n", k=KT)
                         ).then_inc(weights_loaded, 16)
            sp.dma_start(w2_sb[:], w2.rearrange("(k p) n -> p k n", p=P)).then_inc(weights_loaded, 16)
            with nc.allow_non_contiguous_dma(reason="biases and the last layer: 1 K elements in all"):
                sp.dma_start(w3_sb[:], w3.rearrange("(k p) o -> p (k o)", p=P)).then_inc(weights_loaded, 16)
                sp.dma_start(b1_sb[:], b1.rearrange("(k p) -> p k", p=P)).then_inc(weights_loaded, 16)
                sp.dma_start(b2_sb[:], b2.rearrange("(k p) -> p k", p=P)).then_inc(weights_loaded, 16)
            with sp.Fori(1, QUADS) as q:
                for k in range(TQ):
                    sp.wait_ge(gathered[k], 16 * NG * q)
                    sp.dma_start(idx[:, k, :], ids_v[:, bass.ds(TQ * q + k, 1), :]
                                 .rearrange("p a f -> p (a f)")).then_inc(idx_loaded[k], 16)
                    sp.wait_ge(tr_filled, FIRST + NT * TQ * (q - 1) + NT * (k + 1))
                    sp.dma_start(rows[:, k, NG, :], dense_v[:, bass.ds(TQ * q + k, 1), :]
                                 .rearrange("p a f -> p (a f)")).then_inc(dense_loaded[k], 16)
            sp.wait_ge(y_drained, 1 + QUADS)
            sp.dma_start(y.rearrange("b o -> o b"), y_row).then_inc(y_stored, 16)
            sp.wait_ge(y_stored, 16)

        @block.gpsimd
        def _(pool):
            nc.gpsimd.memset(ident[:], 0.0).then_inc(consts_set, 1)
            pool.wait_ge(consts_set, 1)
            nc.gpsimd.affine_select(out=ident[:], in_=ident[:], compare_op=ALU.not_equal, fill=1.0, base=0,
                                    pattern=[[-1, P]], channel_multiplier=1).then_inc(ident_set, 1)
            nc.gpsimd.memset(idsT[:, BATCH:BATCH + QS], 0.0).then_inc(no_ids_set, 1)
            nc.gpsimd.iota(row_i[:], pattern=[[1, CH]], base=0, channel_multiplier=CH).then_inc(rows_numbered, 1)

            def gather(k):
                for n, f in enumerate(GATHERED):
                    nc.gpsimd.indirect_dma_start(
                        rows[:, k, n, :], None, tables[f],
                        bass.IndirectOffsetOnAxis(idx[:, k, f:f + 1], 0)).then_inc(gathered[k], 16)

            for k in range(TQ):
                pool.wait_ge(idx_loaded[k], 16)
                gather(k)
            with pool.Fori(1, QUADS) as q:
                for k in range(TQ):
                    pool.wait_ge(idx_loaded[k], 16 * q + 16)
                    pool.wait_ge(tr_filled, FIRST + NT * TQ * (q - 1) + NT * (k + 1))
                    pool.sem_inc(slot_turned, 1)
                    gather(k)

        @block.vector
        def _(dve):
            for n in range(FIRST):
                nc.vector.memset(gram_bank[n][:], 0.0).then_inc(gram_drained, 1)
            dve.wait_ge(ids_loaded, 16)
            for n, f in enumerate(ONEHOT):
                last = nc.vector.tensor_copy(ids_f[:, :, n], ids_all[:, :, f])
            last.then_inc(ids_cast, 1)
            dve.wait_ge(rows_numbered, 1)
            nc.vector.tensor_copy(row_f[:], row_i[:]).then_inc(row_f_set, 1)
            dve.wait_ge(row_f_set, 1)

            def set_onehot(q, n, chunks):
                for c in chunks:
                    if c == 0:
                        dve.wait_ge(id_filled, NH * q + n + 1)
                    if n >= OB:
                        dve.wait_ge(chunk_done, NH * CH * q + (n - OB) * CH + c + 1)
                    elif c == 0 and not (isinstance(q, int) and q == 0):
                        dve.wait_ge(chunk_done, NH * CH * q)
                    nc.vector.tensor_scalar(onehot[:, n % OB, c, :], id_bank[0:RP, :], row_f[:, c:c + 1],
                                            None, ALU.is_equal).then_inc(onehot_set, 1)

            for n in range(NH):
                dve.wait_ge(part_cast, 2 * n + 1)
                if n:
                    dve.wait_ge(part_taken, 2 * n)
                nc.vector.tensor_tensor(rest, raw[n % 2], split[:, n, 0, :],
                                        ALU.subtract).then_inc(part_taken, 1)
                set_onehot(0, n, range(CH // 2))
                dve.wait_ge(part_cast, 2 * n + 2)
                dve.wait_ge(part_taken, 2 * n + 1)
                nc.vector.tensor_tensor(split[:, n, 2, :], rest, split[:, n, 1, :],
                                        ALU.subtract).then_inc(part_taken, 1)
                set_onehot(0, n, range(CH // 2, CH))
            dve.wait_ge(weights_loaded, 16 * 7)
            nc.vector.tensor_tensor(w1x[:], w1x[:], w1x2, ALU.add).then_inc(w1x_summed, 1)

            def turn(q, k, columns):
                if columns[0] == 0:
                    dve.wait_ge(gram_drained, FIRST + 2 * TQ * q + 2 * k + 2)
                for c in columns:
                    if c:
                        dve.wait_ge(column_turned, (GC - 1) * (TQ * q + k) + c)
                    nc.vector.transpose(pairs[:, k, pairs_of(c, BL)], dots[:, k % 2, :, c]
                                        ).then_inc(column_turned if c < GC - 1 else pairs_set, 1)

            def turn_last(k):
                turned = rows[:, k % 2, :, :].rearrange("p n d -> p (n d)")[:, 0:GC * BL].rearrange("p (c g) -> p c g", c=GC)
                dve.wait_ge(gram_drained, FIRST + 2 * TQ * (QUADS - 1) + 2 * k + 2)
                dve.wait_ge(tr_filled, FIRST + NT * TQ * (QUADS - 1) + NT * (k % 2 + 1))
                dve.wait_ge(pairs_set, TQ * (QUADS - 1) + k)
                nc.vector.transpose(turned, dots[:, k % 2, :, :].rearrange("p i c -> p c i")).then_inc(all_turned, 1)
                dve.wait_ge(all_turned, k)
                for c in range(GC):
                    last = nc.vector.tensor_copy(pairs[:, k, pairs_of(c, c + 1)], turned[:, c, 0:c + 1])
                last.then_inc(pairs_set, 1)

            for n in range(2):
                set_onehot(1, n, range(CH))
            turn(0, 0, range(GC))
            with dve.Fori(0, QUADS - 1) as q:
                turn(q, 1, range(GC))
                set_onehot(q + 1, 2, range(CH))
                turn(q, 2, range(GC))
                set_onehot(q + 1, 3, range(CH))
                turn(q, 3, range(GC))
                for n in range(4, NH):
                    set_onehot(q + 1, n, range(CH))
                for n in range(2):
                    set_onehot(q + 2, n, range(CH))
                turn(q + 1, 0, range(GC))
            for k in range(1, TQ):
                turn_last(k)

        @block.scalar
        def _(act):
            act.wait_ge(ident_set, 1)
            for n in range(NH):
                last = nc.scalar.copy(pick[:, n, :], ident[0:NH, n:n + 1].broadcast_to([NH, P]))
            last.then_inc(pick_set, 1)
            act.sem_inc(y_drained, 1)
            for n in range(FIRST):
                for bank_of, filled, drained, q in ((tr_bank, tr_filled, tr_drained, n),
                                                    (work_bank, work_filled, work_drained, FIRST + n)):
                    act.wait_ge(filled, n + 1)
                    nc.scalar.copy(idsT[:, q * QS:(q + 1) * QS], bank_of[n][0:NH, :]).then_inc(drained, 1)

            def cast_parts(n):
                act.wait_ge(raw_loaded[n % 2], 16 * (n // 2 + 1))
                nc.scalar.copy(split[:, n, 0, :], raw[n % 2]).then_inc(part_cast, 1)
                act.wait_ge(part_taken, 2 * n + 1)
                nc.scalar.copy(split[:, n, 1, :], rest).then_inc(part_cast, 1)

            def drain_sum(use, n):
                act.wait_ge(chunk_done, CH * (use + 1))
                nc.scalar.copy(vecT[:, :, place(ONEHOT[n] + 1)], sum_bank[:]).then_inc(sum_drained, 1)

            def hold_sum(use, q, n):
                act.wait_ge(gram_filled, 2 * TQ * q + 2 * (TQ - 1))
                act.wait_ge(chunk_done, CH * (use + 1))
                nc.scalar.copy(vecT[:, 0:QS - P, place(ONEHOT[n] + 1)], sum_bank[:, 0:QS - P])
                nc.scalar.copy(held[:, n, :], sum_bank[:, QS - P:QS]).then_inc(sum_drained, 1)

            def drain_rows(q, k, i):
                slots, src = TR_BANKS[i], tr_bank[(NT * k + i) % 2]
                act.wait_ge(tr_filled, FIRST + NT * TQ * q + NT * k + i + 1)
                for first, count, low, step in runs(slots):
                    last = nc.scalar.copy(
                        vecT[:, k * P:(k + 1) * P, low:low + step * (count - 1) + 1:step]
                        .rearrange("d s v -> d v s"),
                        src[:, first * P:(first + count) * P].rearrange("d (v s) -> d v s", v=count))
                if i == NT - 1:
                    last = nc.scalar.copy(xT[:, k * P:(k + 1) * P], src[:, (slots.index(NG)) * P:(slots.index(NG) + 1) * P])
                last.then_inc(tr_drained, 1)

            def drain_gram(q, k, h):
                if h == 0 and not (isinstance(q, int) and q == 0 and k < 2):
                    act.wait_ge(pairs_set, TQ * q + k - 1)
                act.wait_ge(gram_filled, 2 * TQ * q + 2 * k + h + 1)
                nc.scalar.copy(dots[:, k % 2, h * HALF:(h + 1) * HALF, :],
                               gram_bank[h][:, 0:HALF * GC].rearrange("p (i f) -> p i f", f=GC)
                               ).then_inc(gram_drained, 1)

            def drain_pairs(first, use, k):
                act.wait_ge(work_filled, first + use + 1)
                nc.scalar.copy(pairsT[0:KP, :, k * P:(k + 1) * P],
                               work_bank[use % 2][0:KP, 0:KT * P].rearrange("m (b s) -> m b s", b=KT)
                               ).then_inc(work_drained, 1)

            def drain_unit(first, use, m, h, b, t0, nt):
                act.wait_ge(work_filled, first + use + 1)
                nc.scalar.activation(h[:, m, t0 * P:(t0 + nt) * P], work_bank[use % 2][:, 0:nt * P], ACT.Relu,
                                     bias=b[:, m:m + 1]).then_inc(work_drained, 1)

            def drain_y(q):
                act.wait_ge(y_filled, q + 1)
                nc.scalar.copy(y_row.rearrange("o (p t) -> o t p", t=TILES)[:, bass.ds(TQ * q, TQ), :],
                               sum_bank[32:33, :].rearrange("o (t p) -> o t p", t=TQ)
                               ).then_inc(y_drained, 1)

            def quad(q):
                first, sums = FIRST + NW * q, NH * (q + 1)
                for at in range(EARLY * CH):
                    if at == ROWS_AT[2]:
                        for h in range(2):
                            drain_gram(q, 1, h)
                        for i in range(NT):
                            drain_rows(q, 2, i)
                        for h in range(2):
                            drain_gram(q, 2, h)
                    if at == ROWS_AT[3]:
                        for i in range(NT):
                            drain_rows(q, 3, i)
                    if at % CH == CH - 1:
                        hold_sum(sums + at // CH, q, at // CH)
                    for k in PAIRS_AFTER.get(at, []):
                        drain_pairs(first, k, k)
                for h in range(2):
                    drain_gram(q, 3, h)
                act.wait_ge(sum_drained, sums + EARLY)
                for n in range(EARLY):
                    nc.scalar.copy(vecT[:, QS - P:QS, place(ONEHOT[n] + 1)], held[:, n, :])
                for at in range(EARLY * CH, NH * CH):
                    if at % CH == CH - 1:
                        drain_sum(sums + at // CH, at // CH)
                    for k in PAIRS_AFTER.get(at, []):
                        drain_pairs(first, k, k)
                for m in range(M1):
                    drain_unit(first, L1 + m, m, h1, b1_sb, 0, TQ)
                    for i in range(2 * m, min(2 * m + 2, NT - 1)):
                        drain_rows(q + 1, 0, i)
                drain_rows(q + 1, 0, NT - 1)
                drain_rows(q + 1, 1, 0)
                for m in range(M2):
                    drain_unit(first, L2 + m, m, h2, b2_sb, 0, TQ)
                    for i in range(1 + 2 * m, 3 + 2 * m):
                        drain_rows(q + 1, 1, i)
                drain_y(q)
                for i in range(1 + 2 * M2, NT):
                    drain_rows(q + 1, 1, i)
                for h in range(2):
                    drain_gram(q + 1, 0, h)

            for n in range(NH):
                cast_parts(n)
                if n:
                    drain_sum(n - 1, n - 1)
                    for i in ROWS_FIRST.get(n - 1, []):
                        drain_rows(0, i // NT, i % NT)
            drain_sum(NH - 1, NH - 1)
            for i in ROWS_FIRST[NH - 1]:
                drain_rows(0, i // NT, i % NT)
            for h in range(2):
                drain_gram(0, 0, h)
            act.wait_ge(weights_loaded, 16 * 7)
            with act.Fori(0, QUADS - 1) as q:
                quad(q)
            q, first = QUADS - 1, FIRST + NW * (QUADS - 1)
            for h in range(2):
                drain_gram(q, 1, h)
            for k in range(2, TQ):
                for i in range(NT):
                    drain_rows(q, k, i)
                    if i == 3:
                        drain_pairs(first, k - 2, k - 2)
                for h in range(2):
                    drain_gram(q, k, h)
            drain_pairs(first, 2, 2)
            use, parts = 3, ((0, TQ - 1), (TQ - 1, 1))
            for t0, nt in parts:
                for m in range(M1):
                    drain_unit(first, use, m, h1, b1_sb, t0, nt)
                    use += 1
                if t0 == 0:
                    drain_pairs(first, use, TQ - 1)
                    use += 1
            for t0, nt in parts:
                for m in range(M2):
                    drain_unit(first, use, m, h2, b2_sb, t0, nt)
                    use += 1
            drain_y(q)

        @block.tensor
        def _(pe):
            pe.wait_ge(ident_set, 1)
            pe.wait_ge(ids_cast, 1)
            for n in range(FIRST):
                for bank_of, filled, q in ((tr_bank, tr_filled, n), (work_bank, work_filled, FIRST + n)):
                    for k in range(TQ):
                        last = nc.tensor.transpose(bank_of[n][0:NH, k * P:(k + 1) * P], ids_f[:, TQ * q + k, :],
                                                   ident[:])
                    last.then_inc(filled, 1)
            pe.wait_ge(pick_set, 1)
            pe.wait_ge(tr_drained, FIRST)
            pe.wait_ge(work_drained, FIRST)

            def spread_ids(q, n):
                nc.tensor.matmul(id_bank[:, :], pick[:, n, :], idsT[:, bass.ds(q * QS, QS)],
                                 start=True, stop=True).then_inc(id_filled, 1)

            def lookup(q, at):
                n, c = at // CH, at % CH
                if c == 0 and n > 0:
                    pe.wait_ge(sum_drained, NH * q + n)
                elif c == 0 and not isinstance(q, int):
                    pe.wait_ge(y_drained, q)
                pe.wait_ge(onehot_set, NH * CH * q + at + 1)
                for part in range(PARTS):
                    last = nc.tensor.matmul(sum_bank[:, :], split[:, n, part, c * DIM:(c + 1) * DIM],
                                            onehot[:, n % OB, c, :],
                                            start=(c == 0 and part == 0), stop=(c == CH - 1 and part == PARTS - 1))
                last.then_inc(chunk_done, 1)

            def ids_used(q, n):
                pe.wait_ge(onehot_set, NH * CH * q + n * CH)

            def lookup_next(q, at):
                n = SPREAD_AFTER.get(at, NH)
                if n < NH:
                    ids_used(q, n)
                lookup(q, at)
                if n < NH:
                    spread_ids(q, n)

            def transpose_rows(q, k, i):
                if i == 0:
                    pe.wait_ge(dense_loaded[k], 16 * q + 16)
                    pe.wait_ge(gathered[k], 16 * NG * q + 16 * NG)
                use = NT * k + i
                pe.wait_ge(tr_drained, FIRST + NT * TQ * q + use - 1)
                for s in TR_BANKS[i]:
                    last = nc.tensor.transpose(tr_bank[use % 2][:, (s % 4) * P:(s % 4 + 1) * P],
                                               rows[:, k, s, :], ident[:])
                last.then_inc(tr_filled, 1)

            def gram(q, k, part, spread=None):
                h, i0 = part // 4, part % 4 * 4
                if part == 0:
                    pe.wait_ge(tr_drained, FIRST + NT * TQ * q + NT * (k + 1))
                if i0 == 0:
                    pe.wait_ge(gram_drained, FIRST + 2 * TQ * q + 2 * k + h - 1)
                if spread is not None:
                    ids_used(q + 1, spread)
                for i in range(i0, i0 + 4):
                    for j in range(4):
                        s = k * P + 32 * j + h * HALF + i
                        last = nc.tensor.matmul(gram_bank[h][32 * j:32 * j + GC, i * GC:(i + 1) * GC],
                                                vecT[:, s, 0:GC], vecT[:, s, 1:VECS], start=True, stop=True)
                if i0 == 12:
                    last.then_inc(gram_filled, 1)
                if spread is not None:
                    spread_ids(q + 1, spread)

            def free_work(first, use):
                pe.wait_ge(work_drained, first + use - 1)

            def transpose_pairs(q, first, use, k):
                pe.wait_ge(pairs_set, TQ * q + k + 1)
                free_work(first, use)
                for b in range(KT):
                    last = nc.tensor.transpose(work_bank[use % 2][0:KP, b * P:(b + 1) * P],
                                               pairs[:, k, PAD + b * KP:PAD + (b + 1) * KP], ident[:])
                last.then_inc(work_filled, 1)

            def layer1(first, use, m, t0, nt):
                if m == 0:
                    pe.wait_ge(work_drained, first + use)
                free_work(first, use + m)
                cols, samples = slice(m * P, (m + 1) * P), slice(t0 * P, (t0 + nt) * P)
                out = work_bank[(use + m) % 2][:, 0:nt * P]
                nc.tensor.matmul(out, w1x[:, cols], xT[:, samples], start=True, stop=False)
                for b in range(KT):
                    last = nc.tensor.matmul(out, w1p[:, b, cols], pairsT[0:KP, b, samples],
                                            start=False, stop=(b == KT - 1))
                last.then_inc(work_filled, 1)

            def layer2(first, use, m, t0, nt):
                if m == 0:
                    pe.wait_ge(work_drained, first + use)
                free_work(first, use + m)
                for b in range(M1):
                    last = nc.tensor.matmul(work_bank[(use + m) % 2][:, 0:nt * P],
                                            w2_sb[:, b, m * P:(m + 1) * P], h1[:, b, t0 * P:(t0 + nt) * P],
                                            start=(b == 0), stop=(b == M1 - 1))
                last.then_inc(work_filled, 1)

            def layer3(first, use):
                pe.wait_ge(work_drained, first + use)
                for b in range(M2):
                    last = nc.tensor.matmul(sum_bank[32:33, :], w3_sb[:, b:b + 1], h2[:, b, :],
                                            start=(b == 0), stop=(b == M2 - 1))
                last.then_inc(y_filled, 1)

            def rows_and_lookups(q, k, at):
                for i in range(NT):
                    transpose_rows(q, k, i)
                    if i % 2 or i == NT - 1:
                        lookup_next(q + 1, at)
                        at += 1
                return at

            def quad(q):
                first = FIRST + NW * q
                for part in range(8):
                    gram(q, 1, part, 2 if part == 0 else None)
                at = rows_and_lookups(q, 2, ROWS_AT[2])
                for part in range(8):
                    gram(q, 2, part)
                while at < EARLY * CH:
                    if at == ROWS_AT[3]:
                        at = rows_and_lookups(q, 3, at)
                    else:
                        lookup_next(q + 1, at)
                        for k in PAIRS_AFTER.get(at, []):
                            transpose_pairs(q, first, k, k)
                        at += 1
                for part in range(8):
                    gram(q, 3, part)
                for at in range(EARLY * CH, NH * CH):
                    lookup_next(q + 1, at)
                    for k in PAIRS_AFTER.get(at, []):
                        transpose_pairs(q, first, k, k)
                for m in range(M1):
                    layer1(first, L1, m, 0, TQ)
                    if m == 0:
                        spread_ids(q + 2, 0)
                    for i in range(2 * m, min(2 * m + 2, NT - 1)):
                        transpose_rows(q + 1, 0, i)
                transpose_rows(q + 1, 0, NT - 1)
                transpose_rows(q + 1, 1, 0)
                for m in range(M2):
                    if m == 0:
                        ids_used(q + 2, 1)
                    layer2(first, L2, m, 0, TQ)
                    if m == 0:
                        spread_ids(q + 2, 1)
                    for i in range(1 + 2 * m, 3 + 2 * m):
                        transpose_rows(q + 1, 1, i)
                pe.wait_ge(sum_drained, NH * (q + 2))
                layer3(first, L2 + M2)
                for i in range(1 + 2 * M2, NT):
                    transpose_rows(q + 1, 1, i)
                for part in range(8):
                    gram(q + 1, 0, part)

            pe.wait_ge(no_ids_set, 1)
            spread_ids(0, 0)
            for n in range(NH):
                pe.wait_ge(part_taken, 2 * n + 2)
                for c in range(CH):
                    if c == CH // 2 and n + 1 < NH:
                        pe.wait_ge(onehot_set, (n + 1) * CH)
                        spread_ids(0, n + 1)
                    lookup(0, n * CH + c)
                if n == NH - 1:
                    spread_ids(1, 0)
                if n in ROWS_FIRST:
                    for i in ROWS_FIRST[n]:
                        transpose_rows(0, i // NT, i % NT)
            pe.wait_ge(sum_drained, NH)
            for part in range(8):
                gram(0, 0, part)
                if part == 3:
                    ids_used(1, 1)
                    spread_ids(1, 1)
            pe.wait_ge(w1x_summed, 1)
            with pe.Fori(0, QUADS - 1) as q:
                quad(q)
            q, first = QUADS - 1, FIRST + NW * (QUADS - 1)
            for part in range(8):
                gram(q, 1, part)
            for k in range(2, TQ):
                for i in range(NT):
                    transpose_rows(q, k, i)
                    if i == 3:
                        transpose_pairs(q, first, k - 2, k - 2)
                for part in range(8):
                    gram(q, k, part)
            transpose_pairs(q, first, 2, 2)
            use, parts = 3, ((0, TQ - 1), (TQ - 1, 1))
            for t0, nt in parts:
                for m in range(M1):
                    layer1(first, use - m, m, t0, nt)
                    use += 1
                if t0 == 0:
                    transpose_pairs(q, first, use, TQ - 1)
                    use += 1
            for t0, nt in parts:
                for m in range(M2):
                    layer2(first, use - m, m, t0, nt)
                    use += 1
            pe.wait_ge(y_drained, q + 1)
            layer3(first, use)


_INS = (["r_dense_features", "ids"] + [f"tbl_{i}" for i in range(FEATS)]
        + ["W_top1", "b_top1", "W_top2", "b_top2", "W_top3"])


def kernel(**inputs):
    import concourse.bacc as bacc
    from concourse.bass_utils import run_bass_kernel_spmd

    nc = bacc.Bacc("TRN2", target_bir_lowering=False, num_devices=1)
    arrays, aps = {}, []
    for name in _INS:
        a = np.ascontiguousarray(inputs[name])
        arrays[f"in_{name}"] = a
        aps.append(nc.dram_tensor(f"in_{name}", a.shape, mybir.dt.from_np(a.dtype), kind="ExternalInput").ap())
    y = nc.dram_tensor("out_y", (BATCH, 1), mybir.dt.float32, kind="ExternalOutput").ap()
    build(nc, aps[0], aps[1], aps[2:2 + FEATS], *aps[2 + FEATS:], y)
    return run_bass_kernel_spmd(nc, [arrays], core_ids=[0]).results[0]["out_y"]
```
